# Optimizing a Trainium2 kernel written in Bass

```python
import numpy as np
import jax
import jax.numpy as jnp

def _softmax(x, axis=-1):
    return jax.nn.softmax(x, axis=axis)

def _gelu(x):
    return jax.nn.gelu(x, approximate=True)

def _silu(x):
    return jax.nn.silu(x)

def _sigmoid(x):
    return jax.nn.sigmoid(x)

def _layernorm(x, axis=-1, eps=1e-05):
    m = jnp.mean(x, axis=axis, keepdims=True)
    v = jnp.var(x, axis=axis, keepdims=True)
    return (x - m) / jnp.sqrt(v + eps)

def _scatter_add(tgt, idx, src, axis=0):
    return tgt.at[idx].add(src)

def _segment_sum(src, seg, n):
    return jax.ops.segment_sum(src, seg, n)
kernel_name = 'mk_adj_resnorm_d1_adj_r2_09bae5'

def setup_inputs(seed: int=0):
    np.random.seed(seed)
    _w = jnp.asarray

    def _rec_inputs():
        import jax
        import jax.numpy as jnp
        _gk = jax.random.key(seed)
        x = -0.0002422 + 1 * jax.random.normal(jax.random.fold_in(_gk, 1), (128, 128, 512), jnp.float32)
        _a = jax.random.bernoulli(jax.random.fold_in(_gk, 2), 0.125, (128, 128, 128))
        _a = jnp.logical_or(_a, jnp.swapaxes(_a, -1, -2))
        _a = jnp.logical_or(_a, jnp.eye(128, dtype=bool))
        adj = _a.astype(jnp.int32)
        return (x, adj)
    x, adj = _rec_inputs()

    def _L0_gnn_setup():
        import jax, jax.numpy as jnp
        import numpy as np
        IN_DIM = 512
        OUT_DIM = 512
        BATCH = 128
        NUM_OBJS = 100
        key = jax.random.key(seed)
        k1, k2, k3, k4, k5 = jax.random.split(key, 5)
        stdv = 1.0 / np.sqrt(OUT_DIM)
        feature = jax.random.normal(k1, (BATCH, NUM_OBJS, IN_DIM), dtype=jnp.float32)
        graph = jax.random.randint(k2, (BATCH, NUM_OBJS, NUM_OBJS), 0, 2, dtype=jnp.int32)
        weight = jax.random.uniform(k3, (IN_DIM, OUT_DIM), dtype=jnp.float32, minval=-stdv, maxval=stdv)
        wq = jax.random.uniform(k4, (IN_DIM, OUT_DIM), dtype=jnp.float32, minval=-stdv, maxval=stdv)
        wk = jax.random.uniform(k5, (IN_DIM, OUT_DIM), dtype=jnp.float32, minval=-stdv, maxval=stdv)
        return {'feature': feature, 'graph': graph, 'weight': weight, 'wq': wq, 'wk': wk}
    _L0_gnn_all = _L0_gnn_setup()
    _L0_gnn_in = {k: v for k, v in _L0_gnn_all.items() if k in ('weight', 'wq', 'wk')}
    del _L0_gnn_all
    return {'x': x, 'adj': adj, 'L0_gnn_weight': _L0_gnn_in['weight'], 'L0_gnn_wq': _L0_gnn_in['wq'], 'L0_gnn_wk': _L0_gnn_in['wk']}

def reference(x, adj, L0_gnn_weight, L0_gnn_wq, L0_gnn_wk):
    import jax
    import jax.numpy as jnp

    def _L0_gnn_ref(feature, graph, weight, wq, wk):
        import jax, jax.numpy as jnp
        import numpy as np
        IN_DIM = 512
        OUT_DIM = 512
        BATCH = 128
        NUM_OBJS = 100
        output = jnp.einsum('bni,io->bno', feature, weight)
        q = jnp.einsum('bni,io->bno', feature, wq)
        k = jnp.einsum('bni,io->bno', feature, wk)
        alpha = jnp.einsum('bno,bmo->bnm', q, k)
        alpha = jnp.maximum(alpha, 0.0) * (graph != 0).astype(alpha.dtype)
        alpha = jax.nn.softmax(alpha, axis=1)
        return jnp.einsum('bnm,bmo->bno', alpha, output)
    x = _layernorm(x + _L0_gnn_ref(x, adj, L0_gnn_weight, L0_gnn_wq, L0_gnn_wk), axis=-1)
    return x

_drawn_inputs = setup_inputs


def setup_inputs(seed=0):
    import zlib

    import numpy as np

    out = dict(_drawn_inputs(seed))
    spreads = {}
    factors = {}
    for name, (base, spread) in spreads.items():
        noise = np.random.default_rng([zlib.crc32(name.encode()), seed]).standard_normal(out[name].shape)
        drawn = base * np.exp(spread * noise) if base else spread * noise
        out[name] = jnp.asarray(drawn.astype(out[name].dtype))
    for name, factor in factors.items():
        out[name] = (out[name] * factor).astype(out[name].dtype)
    return out
```

```python
from contextlib import ExitStack

import concourse.bass as bass
from concourse import mybir

F32 = mybir.dt.float32
F32R = mybir.dt.float32r
I32 = mybir.dt.int32
ALU = mybir.AluOpType
ACT = mybir.ActivationFunctionType
AX_X = mybir.AxisListType.X

P = 128
PACK = 4
EPS = 1e-5


def graph_attention_layernorm(
    nc: bass.Bass,
    xT: bass.AP,
    rows: bass.AP,
    adjT: bass.AP,
    wqkT: bass.AP,
    w: bass.AP,
    out: bass.AP,
):
    GROUPS, _, FREE = xT.shape
    D = w.shape[1] // (FREE // (PACK * P))
    CH = D // P
    N = PACK * P
    assert D == 512 and CH == 4 and FREE == CH * N and GROUPS % 2 == 0
    LEFT = 3 * P

    with ExitStack() as ctx:
        def sb(name, shape, dt):
            return ctx.enter_context(nc.sbuf_tensor(name, shape, dt))

        def psum(name, shape):
            return ctx.enter_context(nc.psum_tensor(name, shape, F32))

        def sem(name):
            return ctx.enter_context(nc.semaphore(name))

        wqk_raw = sb("wqk_raw", [P, CH, 2 * D], F32)
        w_raw = sb("w_raw", [P, CH, D], F32)
        m_hi = sb("m_hi", [P, CH, D], F32R)
        m_lo = sb("m_lo", [P, CH, D], F32R)
        moving_hi = sb("moving_hi", [P, CH, 8, P], F32R)
        moving_lo = sb("moving_lo", [P, CH, 8, P], F32R)
        xT_raw = sb("xT_raw", [P, CH, N], F32)
        x_hi = sb("x_hi", [P, 2, CH, N], F32R)
        x_lo = sb("x_lo", [P, 2, CH, N], F32R)
        v_hi = sb("v_hi", [P, PACK, D], F32R)
        v_lo = sb("v_lo", [P, PACK, D], F32R)
        adj = sb("adj", [P, 2, N], I32)
        mask = sb("mask", [P, N], F32)
        alpha = sb("alpha", [P, PACK, P], F32)
        neg_max = sb("neg_max", [P, PACK], F32)
        exps = sb("exps", [P, PACK, P], F32)
        exp_sum = sb("exp_sum", [P, PACK], F32)
        inv_sum = sb("inv_sum", [P, PACK], F32)
        probs = sb("probs", [P, PACK, P], F32)
        probs_hi = sb("probs_hi", [P, PACK, P], F32R)
        probs_lo = sb("probs_lo", [P, PACK, P], F32R)
        x_rows = sb("x_rows", [P, 2, PACK, D], F32)
        y = sb("y", [P, 2, PACK, D], F32)
        stats = sb("stats", [P, PACK, 6], F32)
        mean_var = sb("mean_var", [P, PACK, 2], F32)
        var_eps = sb("var_eps", [P, PACK], F32)
        eps = sb("eps", [P, PACK], F32)
        minus_half = sb("minus_half", [P, PACK], F32)
        rstd = sb("rstd", [P, PACK], F32)

        q_psum = psum("q_psum", [P, 2, N])
        out_psum = psum("out_psum", [P, 2, D])
        vs_psum = psum("vs_psum", [P, 2, 1024])
        V0, S0 = P, P + D

        wqk_loaded = [sem(f"wqk_loaded{c}") for c in range(CH)]
        w_loaded = sem("w_loaded")
        xT_loaded = sem("xT_loaded")
        adj_loaded = [sem(f"adj_loaded{s}") for s in range(2)]
        rows_loaded = [sem(f"rows_loaded{s}") for s in range(2)]
        y_stored = [sem(f"y_stored{s}") for s in range(2)]
        m_summed = sem("m_summed")
        m_hi_done = sem("m_hi_done")
        m_lo_done = sem("m_lo_done")
        w_hi_done = sem("w_hi_done")
        w_lo_done = sem("w_lo_done")
        x_hi_done = sem("x_hi_done")
        x_lo_done = sem("x_lo_done")
        q_summed = sem("q_summed")
        q_hi_done = sem("q_hi_done")
        q_lo_done = sem("q_lo_done")
        vs_summed = sem("vs_summed")
        v_hi_done = sem("v_hi_done")
        v_lo_done = sem("v_lo_done")
        alpha_done = sem("alpha_done")
        mask_done = sem("mask_done")
        neg_max_done = sem("neg_max_done")
        exps_done = sem("exps_done")
        inv_sum_done = sem("inv_sum_done")
        probs_done = sem("probs_done")
        probs_hi_done = sem("probs_hi_done")
        probs_lo_done = sem("probs_lo_done")
        out_summed = sem("out_summed")
        h_done = sem("h_done")
        stats_done = sem("stats_done")
        mean_var_done = sem("mean_var_done")
        constants_set = sem("constants_set")
        var_eps_done = sem("var_eps_done")
        rstd_done = sem("rstd_done")
        y_done = sem("y_done")

        def f32(ap):
            return ap.bitcast(F32)

        def reached(eng, semaphore, count):
            if isinstance(count, int) and count <= 0:
                return
            eng.wait_ge(semaphore, count)

        def over_groups(eng, phase):
            phase(0, -1, 1)
            phase(1, 0, 0)
            phase(2, 0, 1)
            with eng.Fori(1, GROUPS // 2 - 1) as p:
                phase(2 * p + 1, p, 0)
                phase(2 * p + 2, p, 1)
            last = GROUPS // 2 - 1
            phase(GROUPS - 1, last, 0)
            phase(GROUPS, last, 1)

        def is_first(g):
            return isinstance(g, int) and g == 0

        def is_past(g):
            return isinstance(g, int) and g >= GROUPS

        block = ctx.enter_context(nc.Block())

        @block.sync
        def _(sp):
            def load_xT(g):
                reached(sp, x_hi_done, CH * g)
                reached(sp, x_lo_done, CH * g)
                sp.dma_start(xT_raw[:, :, :].rearrange("p c n -> p (c n)"), xT[g, :, :]).then_inc(xT_loaded, 16)

            for c in range(CH):
                sp.dma_start(wqk_raw[:, c, :], wqkT[c, :, :]).then_inc(wqk_loaded[c], 16)
            load_xT(0)
            sp.dma_start(w_raw[:, :, :].rearrange("p c n -> p (c n)"), w).then_inc(w_loaded, 16)
            sp.dma_start(adj[:, 0, :], adjT[0, :, :]).then_inc(adj_loaded[0], 16)
            load_xT(1)

            def phase(g, p, k):
                slot, other = 1 - k, k
                if not is_past(g):
                    if not (isinstance(g, int) and g + 1 >= GROUPS):
                        reached(sp, mask_done, g)
                        sp.dma_start(adj[:, other, :], adjT[g + 1, :, :]).then_inc(adj_loaded[other], 16)
                    reached(sp, h_done, PACK * (g - 1))
                    sp.dma_start(x_rows[:, slot, :, :].rearrange("p e d -> p (e d)"),
                                 rows[g, :, :]).then_inc(rows_loaded[slot], 16)
                    if not (isinstance(g, int) and g + 2 >= GROUPS):
                        load_xT(g + 2)
                if not is_first(g):
                    sp.wait_ge(y_done, PACK * g)
                    sp.dma_start(out[g - 1, :, :],
                                 y[:, other, :, :].rearrange("p e d -> p (e d)")).then_inc(y_stored[other], 16)

            phase(0, -1, 1)
            phase(1, 0, 0)
            phase(2, 0, 1)
            with sp.Fori(1, GROUPS // 2 - 2) as p:
                phase(2 * p + 1, p, 0)
                phase(2 * p + 2, p, 1)
            for g in range(GROUPS - 3, GROUPS + 1):
                phase(g, (g - 1) // 2, (g - 1) % 2)
            for s in range(2):
                sp.wait_ge(y_stored[s], 16 * GROUPS // 2)

        @block.tensor
        def _(pe):
            m_banks = [q_psum[:, 0, :], q_psum[:, 1, :], out_psum[:, 0, :], out_psum[:, 1, :]]
            for j in range(CH):
                pe.wait_ge(wqk_loaded[j], 16)
                for i in range(CH):
                    mm = nc.tensor.matmul(m_banks[i], wqk_raw[:, j, i * P:(i + 1) * P],
                                          wqk_raw[:, j, D:2 * D], start=(j == 0), stop=(j == CH - 1))
                    if j == CH - 1:
                        mm.then_inc(m_summed, 1)

            def project(g, slot, o):
                bank = q_psum[:, o % 2, :]
                if is_first(g):
                    pe.wait_ge(m_lo_done, CH)
                    if o == 0:
                        pe.wait_ge(x_hi_done, CH)
                        pe.wait_ge(x_lo_done, CH)
                elif o == 0:
                    pe.wait_ge(x_hi_done, CH * (g + 1))
                    pe.wait_ge(x_lo_done, CH * (g + 1))
                reached(pe, q_lo_done, CH * g + o - 1)
                n = 0
                for i in range(CH):
                    for weights, data in ((m_hi, x_hi), (m_hi, x_lo), (m_lo, x_hi)):
                        mm = nc.tensor.matmul(bank, weights[:, i, o * P:(o + 1) * P], data[:, slot, i, :],
                                              start=(n == 0), stop=(n == 3 * CH - 1))
                        n += 1
                mm.then_inc(q_summed, 1)

            def values_scores(g, slot, e):
                pair = vs_psum[:, e % 2, :]
                if is_first(g) and e == 0:
                    pe.wait_ge(w_hi_done, 1)
                    pe.wait_ge(w_lo_done, 1)
                reached(pe, alpha_done, PACK * g + e - 1)
                n = 0
                for i in range(CH):
                    for data, mov in ((x_hi, moving_hi), (x_hi, moving_lo), (x_lo, moving_hi)):
                        nc.tensor.matmul(pair[:, V0:V0 + LEFT], data[:, slot, i, e * P:(e + 1) * P],
                                         mov[:, i, 0:3, :], start=(n == 0), stop=(n == 3 * CH - 1))
                        n += 1
                if e == 0:
                    pe.wait_ge(q_lo_done, CH * (g + 1))
                n = 0
                for i in range(CH):
                    for data, mov in ((x_hi, moving_hi), (x_hi, moving_lo), (x_lo, moving_hi)):
                        mm = nc.tensor.matmul(pair[:, V0 + LEFT:S0 + P], data[:, slot, i, e * P:(e + 1) * P],
                                              mov[:, i, 3:5 + e:1 + e, :], start=(n == 0), stop=(n == 3 * CH - 1))
                        n += 1
                mm.then_inc(vs_summed, 1)

            def attend(g, e):
                if e == 0:
                    pe.wait_ge(probs_lo_done, g + 1)
                if is_first(g) and e < 2:
                    pass
                else:
                    pe.wait_ge(h_done, PACK * g + e - 1)
                n = 0
                for pr, v in ((probs_hi, v_hi), (probs_hi, v_lo), (probs_lo, v_hi)):
                    mm = nc.tensor.matmul(out_psum[:, e % 2, :], pr[:, e, :], v[:, e, :],
                                          start=(n == 0), stop=(n == 2))
                    n += 1
                mm.then_inc(out_summed, 1)

            def phase(g, p, k):
                slot = 1 - k
                if is_past(g):
                    for e in range(PACK):
                        attend(g - 1, e)
                    return
                for o in range(3):
                    project(g, slot, o)
                if not is_first(g):
                    attend(g - 1, 0)
                    attend(g - 1, 1)
                project(g, slot, 3)
                if not is_first(g):
                    attend(g - 1, 2)
                    attend(g - 1, 3)
                for e in range(PACK):
                    values_scores(g, slot, e)

            over_groups(pe, phase)

        @block.scalar
        def _(act):
            def split_x(g, slot, c):
                if c == 0:
                    act.wait_ge(xT_loaded, 16 * (g + 1))
                    reached(act, vs_summed, PACK * (g - 1))
                nc.scalar.activation(x_hi[:, slot, c, :], xT_raw[:, c, :], ACT.Copy).then_inc(x_hi_done, 1)

            def split_q(g, o):
                act.wait_ge(q_summed, CH * g + o + 1)
                nc.scalar.activation(moving_hi[:, o, 4:8, :], q_psum[:, o % 2, :].rearrange("p (e n) -> p e n", n=P),
                                     ACT.Copy).then_inc(q_hi_done, 1)

            def split_v(g, e):
                act.wait_ge(vs_summed, PACK * g + e + 1)
                nc.scalar.activation(v_hi[:, e, :], vs_psum[:, e % 2, V0:V0 + D], ACT.Copy).then_inc(v_hi_done, 1)

            def exponentials(g):
                act.wait_ge(neg_max_done, g + 1)
                reached(act, probs_done, g)
                for e in range(PACK):
                    nc.scalar.activation(exps[:, e, :], alpha[:, e, :], ACT.Exp, bias=neg_max[:, e:e + 1],
                                         accum_out=exp_sum[:, e:e + 1]).then_inc(exps_done, 1)

            def split_probs(g):
                act.wait_ge(probs_done, g + 1)
                reached(act, out_summed, PACK * g)
                nc.scalar.activation(probs_hi[:, :, :], probs[:, :, :], ACT.Copy).then_inc(probs_hi_done, 1)

            for c in range(CH):
                split_x(0, 0, c)
            for i, bank in enumerate([q_psum[:, 0, :], q_psum[:, 1, :], out_psum[:, 0, :], out_psum[:, 1, :]]):
                act.wait_ge(m_summed, i + 1)
                nc.scalar.activation(m_hi[:, i, :], bank, ACT.Copy).then_inc(m_hi_done, 1)
            act.wait_ge(w_loaded, 16)
            nc.scalar.activation(moving_hi[:, :, 0:4, :], w_raw[:, :, :].rearrange("p c (k n) -> p c k n", n=P),
                                 ACT.Copy).then_inc(w_hi_done, 1)

            def phase(g, p, k):
                slot, other = 1 - k, k
                if not is_first(g):
                    exponentials(g - 1)
                if not is_past(g):
                    split_q(g, 0)
                if not is_first(g):
                    split_probs(g - 1)
                if is_past(g):
                    return
                more = not (isinstance(g, int) and g + 1 >= GROUPS)
                split_q(g, 1)
                split_q(g, 2)
                if more:
                    split_x(g + 1, other, 0)
                    split_x(g + 1, other, 1)
                split_q(g, 3)
                if more:
                    split_x(g + 1, other, 2)
                    split_x(g + 1, other, 3)
                for e in range(PACK):
                    split_v(g, e)

            over_groups(act, phase)

        @block.gpsimd
        def _(pool):
            def split_x(g, slot, c):
                pool.wait_ge(x_hi_done, CH * g + c + 1)
                nc.gpsimd.tensor_tensor(x_lo[:, slot, c, :], xT_raw[:, c, :], f32(x_hi[:, slot, c, :]),
                                        ALU.subtract).then_inc(x_lo_done, 1)

            def inverse_deviation(g):
                pool.wait_ge(mean_var_done, PACK * (g + 1))
                reached(pool, y_done, PACK * g)
                nc.gpsimd.tensor_tensor(var_eps[:, :], mean_var[:, :, 1], eps[:, :], ALU.add).then_inc(var_eps_done, 1)
                pool.wait_ge(var_eps_done, g + 1)
                nc.gpsimd.tensor_tensor(rstd[:, :], var_eps[:, :], minus_half[:, :], ALU.pow).then_inc(rstd_done, 1)

            nc.gpsimd.memset(eps[:, :], EPS).then_inc(constants_set, 1)
            nc.gpsimd.memset(minus_half[:, :], -0.5).then_inc(constants_set, 1)
            pool.wait_ge(constants_set, 2)
            for c in range(CH):
                split_x(0, 0, c)
            pool.wait_ge(w_hi_done, 1)
            nc.gpsimd.tensor_tensor(moving_lo[:, :, 0:4, :], w_raw[:, :, :].rearrange("p c (k n) -> p c k n", n=P),
                                    f32(moving_hi[:, :, 0:4, :]), ALU.subtract).then_inc(w_lo_done, 1)

            def phase(g, p, k):
                if not is_past(g) and not (isinstance(g, int) and g + 1 >= GROUPS):
                    for c in range(CH):
                        split_x(g + 1, k, c)
                if not is_first(g):
                    inverse_deviation(g - 1)

            over_groups(pool, phase)

        @block.vector
        def _(dve):
            def make_mask(g, slot, loads):
                reached(dve, stats_done, PACK * g)
                dve.wait_ge(adj_loaded[slot], 16 * loads)
                reached(dve, alpha_done, PACK * g)
                nc.vector.tensor_scalar(mask[:, :], adj[:, slot, :], 0.0, None, ALU.not_equal).then_inc(mask_done, 1)

            def split_q(g, o):
                dve.wait_ge(q_hi_done, CH * g + o + 1)
                nc.vector.tensor_tensor(moving_lo[:, o, 4:8, :], q_psum[:, o % 2, :].rearrange("p (e n) -> p e n", n=P),
                                        f32(moving_hi[:, o, 4:8, :]), ALU.subtract).then_inc(q_lo_done, 1)

            def split_v_and_mask_scores(g, e):
                dve.wait_ge(v_hi_done, PACK * g + e + 1)
                nc.vector.tensor_tensor(v_lo[:, e, :], vs_psum[:, e % 2, V0:V0 + D], f32(v_hi[:, e, :]),
                                        ALU.subtract).then_inc(v_lo_done, 1)
                if e == 0:
                    dve.wait_ge(mask_done, g + 1)
                    reached(dve, exps_done, PACK * g)
                nc.vector.scalar_tensor_tensor(alpha[:, e, :], vs_psum[:, e % 2, S0:S0 + P], 0.0,
                                               mask[:, e * P:(e + 1) * P], ALU.max, ALU.mult).then_inc(alpha_done, 1)

            def row_max(g):
                dve.wait_ge(alpha_done, PACK * (g + 1))
                nc.vector.tensor_reduce(neg_max[:, :], alpha[:, :, :], AX_X, ALU.max, negate=True).then_inc(neg_max_done, 1)

            def normalise_probs(g):
                dve.wait_ge(exps_done, PACK * (g + 1))
                nc.vector.reciprocal(inv_sum[:, :], exp_sum[:, :]).then_inc(inv_sum_done, 1)
                dve.wait_ge(inv_sum_done, g + 1)
                nc.vector.tensor_tensor(probs[:, :, :], exps[:, :, :],
                                        inv_sum[:, :].unsqueeze(2).to_broadcast([P, PACK, P]),
                                        ALU.mult).then_inc(probs_done, 1)

            def split_probs(g):
                dve.wait_ge(probs_hi_done, g + 1)
                nc.vector.tensor_tensor(probs_lo[:, :, :], probs[:, :, :], f32(probs_hi[:, :, :]),
                                        ALU.subtract).then_inc(probs_lo_done, 1)

            def residual(g, slot, e, half):
                if e == 0:
                    dve.wait_ge(rows_loaded[slot], 16 * (half + 1))
                    reached(dve, y_stored[slot], 16 * half)
                dve.wait_ge(out_summed, PACK * g + e + 1)
                nc.vector.tensor_tensor(y[:, slot, e, :], out_psum[:, e % 2, :], x_rows[:, slot, e, :],
                                        ALU.add).then_inc(h_done, 1)

            def statistics(g, slot, e):
                dve.wait_ge(h_done, PACK * g + e + 1)
                nc.vector.bn_stats(stats[:, e, :], y[:, slot, e, :]).then_inc(stats_done, 1)

            def mean_variance(g):
                for e in range(PACK):
                    nc.vector.bn_aggr(mean_var[:, e, :], stats[:, e, :]).then_inc(mean_var_done, 1)

            def normalise(g, slot):
                dve.wait_ge(rstd_done, g + 1)
                for e in range(PACK):
                    nc.vector.tensor_scalar(y[:, slot, e, :], y[:, slot, e, :], mean_var[:, e, 0:1], rstd[:, e:e + 1],
                                            ALU.subtract, ALU.mult).then_inc(y_done, 1)

            for i, bank in enumerate([q_psum[:, 0, :], q_psum[:, 1, :], out_psum[:, 0, :], out_psum[:, 1, :]]):
                dve.wait_ge(m_hi_done, i + 1)
                nc.vector.tensor_tensor(m_lo[:, i, :], bank, f32(m_hi[:, i, :]), ALU.subtract).then_inc(m_lo_done, 1)

            def phase(g, p, k):
                slot, other = 1 - k, k
                behind, ahead = not is_first(g), not is_past(g)
                if behind:
                    row_max(g - 1)
                if ahead:
                    split_q(g, 0)
                if behind:
                    normalise_probs(g - 1)
                    split_probs(g - 1)
                if ahead:
                    split_q(g, 1)
                    split_q(g, 2)
                if behind:
                    residual(g - 1, other, 0, p)
                    residual(g - 1, other, 1, p)
                    statistics(g - 1, other, 0)
                    statistics(g - 1, other, 1)
                if ahead:
                    split_q(g, 3)
                if behind:
                    residual(g - 1, other, 2, p)
                    residual(g - 1, other, 3, p)
                    statistics(g - 1, other, 2)
                    statistics(g - 1, other, 3)
                if ahead:
                    make_mask(g, slot, p + k + 1)
                else:
                    dve.wait_ge(stats_done, PACK * g)
                if behind:
                    mean_variance(g - 1)
                if ahead:
                    split_v_and_mask_scores(g, 0)
                if behind:
                    normalise(g - 1, other)
                if ahead:
                    for e in range(1, PACK):
                        split_v_and_mask_scores(g, e)

            over_groups(dve, phase)


def kernel(x, adj, L0_gnn_weight, L0_gnn_wq, L0_gnn_wk):
    import numpy as np
    import concourse.bacc as bacc
    from concourse.bass_utils import run_bass_kernel_spmd

    x, adj = np.asarray(x), np.asarray(adj)
    B, R, D = x.shape
    G, CH = B // PACK, D // P
    assert R == P and B % (2 * PACK) == 0
    xT = x.reshape(G, PACK, R, CH, P).transpose(0, 4, 3, 1, 2).reshape(G, P, CH * PACK * R)
    rows = x.reshape(G, PACK, R, D).transpose(0, 2, 1, 3).reshape(G, R, PACK * D)
    adjT = adj.reshape(G, PACK, R, R).transpose(0, 3, 1, 2).reshape(G, R, PACK * R)
    wqkT = np.concatenate([np.asarray(L0_gnn_wq).T.reshape(CH, P, D), np.asarray(L0_gnn_wk).T.reshape(CH, P, D)], axis=2)
    w = np.asarray(L0_gnn_weight).reshape(CH, P, D).transpose(1, 0, 2).reshape(P, CH * D)

    nc = bacc.Bacc("TRN2", target_bir_lowering=False, num_devices=1)
    arrays, args = {}, []
    for name, a in (("xT", xT), ("rows", rows), ("adjT", adjT), ("wqkT", wqkT), ("w", w)):
        arrays[name] = np.ascontiguousarray(a)
        args.append(nc.dram_tensor(name, a.shape, mybir.dt.from_np(a.dtype), kind="ExternalInput").ap())
    args.append(nc.dram_tensor("y_rows", (G, R, PACK * D), F32, kind="ExternalOutput").ap())
    graph_attention_layernorm(nc, *args)
    result = run_bass_kernel_spmd(nc, [arrays], core_ids=[0])
    y_rows = result.results[0]["y_rows"]
    return y_rows.reshape(G, R, PACK, D).transpose(0, 2, 1, 3).reshape(B, R, D)
```

```python
from contextlib import ExitStack

import concourse.bass as bass
from concourse import mybir

F32 = mybir.dt.float32
F32R = mybir.dt.float32r
I32 = mybir.dt.int32
ALU = mybir.AluOpType
ACT = mybir.ActivationFunctionType
AX_X = mybir.AxisListType.X

P = 128
PACK = 4
EPS = 1e-5
WARM_UP = 6


def graph_attention_layernorm(
    nc: bass.Bass,
    xT: bass.AP,
    rows: bass.AP,
    adjT: bass.AP,
    wqkT: bass.AP,
    w: bass.AP,
    out: bass.AP,
):
    GROUPS, _, FREE = xT.shape
    D = w.shape[1] // (FREE // (PACK * P))
    CH = D // P
    N = PACK * P
    assert D == 512 and CH == 4 and FREE == CH * N and GROUPS % 2 == 0
    LEFT = 3 * P

    with ExitStack() as ctx:
        def sb(name, shape, dt):
            return ctx.enter_context(nc.sbuf_tensor(name, shape, dt))

        def psum(name, shape):
            return ctx.enter_context(nc.psum_tensor(name, shape, F32))

        def sem(name):
            return ctx.enter_context(nc.semaphore(name))

        wqk_hi = sb("wqk_hi", [P, CH - 1, 2 * D], F32R)
        wqk_lo = sb("wqk_lo", [P, CH - 1, 2 * D], F32R)
        warm = sb("warm", [P, D], mybir.dt.bfloat16)
        w_raw = sb("w_raw", [P, CH, D], F32)
        m_hi = sb("m_hi", [P, CH, D], F32R)
        m_lo = sb("m_lo", [P, CH, D], F32R)
        moving_hi = sb("moving_hi", [P, CH, 8, P], F32R)
        moving_lo = sb("moving_lo", [P, CH, 8, P], F32R)
        xT_raw = sb("xT_raw", [P, CH, N], F32)
        x_hi = sb("x_hi", [P, 2, CH, N], F32R)
        x_lo = sb("x_lo", [P, 2, CH, N], F32R)
        v_hi = sb("v_hi", [P, PACK, D], F32R)
        v_lo = sb("v_lo", [P, PACK, D], F32R)
        adj = sb("adj", [P, 2, N], I32)
        mask = sb("mask", [P, N], F32)
        alpha = sb("alpha", [P, PACK, P], F32)
        neg_max = sb("neg_max", [P, PACK], F32)
        exps = sb("exps", [P, PACK, P], F32)
        exp_sum = sb("exp_sum", [P, PACK], F32)
        inv_sum = sb("inv_sum", [P, PACK], F32)
        probs_hi = sb("probs_hi", [P, PACK, P], F32R)
        probs_lo = sb("probs_lo", [P, PACK, P], F32R)
        x_rows = sb("x_rows", [P, 2, PACK, D], F32)
        y = sb("y", [P, 2, PACK, D], F32)
        wqk_raw = y[:, :, :, :].rearrange("p s (h e) d -> p (s h) (e d)", h=2)
        stats = sb("stats", [P, PACK, 6], F32)
        mean_var = sb("mean_var", [P, PACK, 2], F32)
        var_eps = sb("var_eps", [P, PACK], F32)
        eps = sb("eps", [P, 1], F32)
        minus_half = sb("minus_half", [P, 1], F32)
        rstd = sb("rstd", [P, PACK], F32)

        q_psum = psum("q_psum", [P, 2, N])
        out_psum = psum("out_psum", [P, 2, D])
        vs_psum = psum("vs_psum", [P, 2, 1024])
        V0, S0 = P, P + D

        wqk_loaded = [sem(f"wqk_loaded{c}") for c in range(CH)]
        w_loaded = sem("w_loaded")
        xT_loaded = sem("xT_loaded")
        adj_loaded = [sem(f"adj_loaded{s}") for s in range(2)]
        rows_loaded = [sem(f"rows_loaded{s}") for s in range(2)]
        y_stored = [sem(f"y_stored{s}") for s in range(2)]
        wqk_hi_done = sem("wqk_hi_done")
        wqk_lo_done = sem("wqk_lo_done")
        m_summed = sem("m_summed")
        m_hi_done = sem("m_hi_done")
        m_lo_done = sem("m_lo_done")
        w_hi_done = sem("w_hi_done")
        w_lo_done = sem("w_lo_done")
        x_hi_done = sem("x_hi_done")
        x_lo_done = sem("x_lo_done")
        q_summed = sem("q_summed")
        q_hi_done = sem("q_hi_done")
        q_lo_done = sem("q_lo_done")
        mask_done = sem("mask_done")
        left_summed = sem("left_summed")
        right_summed = sem("right_summed")
        v_hi_done = sem("v_hi_done")
        v_lo_done = sem("v_lo_done")
        alpha_done = sem("alpha_done")
        neg_max_done = sem("neg_max_done")
        exps_done = sem("exps_done")
        inv_sum_done = sem("inv_sum_done")
        probs_hi_done = sem("probs_hi_done")
        probs_lo_done = sem("probs_lo_done")
        out_summed = sem("out_summed")
        h_done = sem("h_done")
        stats_done = sem("stats_done")
        mean_var_done = sem("mean_var_done")
        var_eps_done = sem("var_eps_done")
        rstd_done = sem("rstd_done")
        y_done = sem("y_done")
        constants_set = sem("constants_set")
        warm_set = sem("warm_set")
        last_stored = sem("last_stored")

        def f32(ap):
            return ap.bitcast(F32)

        def reached(eng, semaphore, count):
            if isinstance(count, int) and count <= 0:
                return
            eng.wait_ge(semaphore, count)

        def steady_loop(engine_type, end):
            return nc.Fori(1, end, engines=(engine_type,), hint_back_edge=True)

        def over_groups(engine_type, phase):
            phase(0, -1, 1)
            phase(1, 0, 0)
            phase(2, 0, 1)
            with steady_loop(engine_type, GROUPS // 2 - 1) as p:
                phase(2 * p + 1, p, 0)
                phase(2 * p + 2, p, 1)
            last = GROUPS // 2 - 1
            phase(GROUPS - 1, last, 0)
            phase(GROUPS, last, 1)

        def is_first(g):
            return isinstance(g, int) and g == 0

        def is_past(g):
            return isinstance(g, int) and g >= GROUPS

        def count(g, e):
            return PACK * g + e + 1

        m_banks = [q_psum[:, 0, :], q_psum[:, 1, :], out_psum[:, 0, :], out_psum[:, 1, :]]
        block = ctx.enter_context(nc.Block())

        @block.sync
        def _(sp):
            def load_xT(g):
                reached(sp, x_hi_done, CH * g)
                reached(sp, x_lo_done, CH * g)
                sp.dma_start(xT_raw[:, :, :].rearrange("p c n -> p (c n)"), xT[g, :, :]).then_inc(xT_loaded, 16)

            def load_rows(g, slot):
                sp.dma_start(x_rows[:, slot, :, :].rearrange("p e d -> p (e d)"),
                             rows[g, :, :]).then_inc(rows_loaded[slot], 16)

            for c in range(CH):
                sp.dma_start(wqk_raw[:, c, :], wqkT[c, :, :]).then_inc(wqk_loaded[c], 16)
            load_xT(0)
            sp.dma_start(w_raw[:, :, :].rearrange("p c n -> p (c n)"), w).then_inc(w_loaded, 16)
            sp.dma_start(adj[:, 0, :], adjT[0, :, :]).then_inc(adj_loaded[0], 16)
            load_rows(0, 0)
            load_xT(1)

            def phase(g, p, k):
                slot, other = 1 - k, k
                if not (isinstance(g, int) and g + 1 >= GROUPS):
                    reached(sp, mask_done, g)
                    sp.dma_start(adj[:, other, :], adjT[g + 1, :, :]).then_inc(adj_loaded[other], 16)
                    reached(sp, h_done, PACK * g)
                    load_rows(g + 1, other)
                if not is_first(g) and not is_past(g):
                    sp.wait_ge(y_done, PACK * g)
                    sp.dma_start(out[g - 1, :, :],
                                 y[:, other, :, :].rearrange("p e d -> p (e d)")).then_inc(y_stored[other], 16)
                if not (isinstance(g, int) and g + 2 >= GROUPS):
                    load_xT(g + 2)

            phase(0, -1, 1)
            phase(1, 0, 0)
            phase(2, 0, 1)
            with steady_loop(mybir.EngineType.SP, GROUPS // 2 - 2) as p:
                phase(2 * p + 1, p, 0)
                phase(2 * p + 2, p, 1)
            for g in range(GROUPS - 3, GROUPS):
                phase(g, (g - 1) // 2, (g - 1) % 2)
            for e in range(PACK):
                sp.wait_ge(y_done, count(GROUPS - 1, e))
                sp.dma_start(out[GROUPS - 1, :, e * D:(e + 1) * D], y[:, 1, e, :]).then_inc(last_stored, 16)
            sp.wait_ge(y_stored[0], 16 * (GROUPS // 2))
            sp.wait_ge(y_stored[1], 16 * (GROUPS // 2 - 1))
            sp.wait_ge(last_stored, 16 * PACK)

        @block.tensor
        def _(pe):
            pe.wait_ge(warm_set, 1)
            for n in range(WARM_UP):
                nc.tensor.matmul(vs_psum[:, 0, 0:D], warm[:, 0:P], warm[:, :], start=True, stop=True)

            pe.wait_ge(wqk_loaded[0], 16)
            for i in range(CH):
                nc.tensor.matmul(m_banks[i], wqk_raw[:, 0, i * P:(i + 1) * P], wqk_raw[:, 0, D:2 * D],
                                 start=True, stop=False)
            for j in range(CH - 1):
                pe.wait_ge(wqk_lo_done, j + 1)
                for i in range(CH):
                    for n, (a, b) in enumerate(((wqk_hi, wqk_hi), (wqk_hi, wqk_lo), (wqk_lo, wqk_hi))):
                        mm = nc.tensor.matmul(m_banks[i], a[:, j, i * P:(i + 1) * P], b[:, j, D:2 * D],
                                              start=False, stop=(j == CH - 2 and n == 2))
                    if j == CH - 2:
                        mm.then_inc(m_summed, 1)

            def project(g, slot, o):
                bank = q_psum[:, o % 2, :]
                if o == 0 and not is_first(g):
                    pe.wait_ge(x_lo_done, CH * (g + 1))
                reached(pe, q_lo_done, CH * g + o - 1)
                n = 0
                for i in range(CH):
                    if is_first(g) and o == 0:
                        pe.wait_ge(m_lo_done, i + 1)
                        pe.wait_ge(x_lo_done, i + 1)
                    for weights, data in ((m_hi, x_hi), (m_hi, x_lo), (m_lo, x_hi)):
                        mm = nc.tensor.matmul(bank, weights[:, i, o * P:(o + 1) * P], data[:, slot, i, :],
                                              start=(n == 0), stop=(n == 3 * CH - 1))
                        n += 1
                mm.then_inc(q_summed, 1)

            def pair_is_free(g, e):
                reached(pe, v_lo_done, PACK * g + e - 1)

            def left(g, slot, e):
                n = 0
                for i in range(CH):
                    for data, mov in ((x_hi, moving_hi), (x_hi, moving_lo), (x_lo, moving_hi)):
                        mm = nc.tensor.matmul(vs_psum[:, e % 2, V0:V0 + LEFT], data[:, slot, i, e * P:(e + 1) * P],
                                              mov[:, i, 0:3, :], start=(n == 0), stop=(n == 3 * CH - 1))
                        n += 1
                mm.then_inc(left_summed, 1)

            def right(g, slot, e):
                n = 0
                for i in range(CH):
                    for data, mov in ((x_hi, moving_hi), (x_hi, moving_lo), (x_lo, moving_hi)):
                        mm = nc.tensor.matmul(vs_psum[:, e % 2, V0 + LEFT:S0 + P], data[:, slot, i, e * P:(e + 1) * P],
                                              mov[:, i, 3:5 + e:1 + e, :], start=(n == 0), stop=(n == 3 * CH - 1))
                        n += 1
                mm.then_inc(right_summed, 1)

            def attend(g, e):
                pe.wait_ge(probs_lo_done, count(g, e))
                pe.wait_ge(v_lo_done, count(g, e))
                reached(pe, h_done, PACK * g + e - 1)
                for n, (pr, v) in enumerate(((probs_hi, v_hi), (probs_hi, v_lo), (probs_lo, v_hi))):
                    mm = nc.tensor.matmul(out_psum[:, e % 2, :], pr[:, e, :], v[:, e, :],
                                          start=(n == 0), stop=(n == 2))
                mm.then_inc(out_summed, 1)

            def phase(g, p, k):
                slot = 1 - k
                if is_past(g):
                    attend(g - 1, 3)
                    return
                project(g, slot, 0)
                if not is_first(g):
                    attend(g - 1, 3)
                for o in range(1, CH):
                    project(g, slot, o)
                if is_first(g):
                    pe.wait_ge(w_lo_done, CH)
                pair_is_free(g, 0)
                left(g, slot, 0)
                pe.wait_ge(q_lo_done, CH * (g + 1))
                right(g, slot, 0)
                for e in range(1, PACK):
                    pair_is_free(g, e)
                    right(g, slot, e)
                    left(g, slot, e)
                    attend(g, e - 1)

            over_groups(mybir.EngineType.PE, phase)

        @block.scalar
        def _(act):
            def split_x(g, slot, c):
                if c == 0:
                    act.wait_ge(xT_loaded, 16 * (g + 1))
                    reached(act, left_summed, PACK * (g - 1))
                nc.scalar.activation(x_hi[:, slot, c, :], xT_raw[:, c, :], ACT.Copy).then_inc(x_hi_done, 1)

            def split_q(g, o):
                act.wait_ge(q_summed, CH * g + o + 1)
                nc.scalar.activation(moving_hi[:, o, 4:8, :], q_psum[:, o % 2, :].rearrange("p (e n) -> p e n", n=P),
                                     ACT.Copy).then_inc(q_hi_done, 1)

            def split_v(g, e):
                act.wait_ge(left_summed, count(g, e))
                act.wait_ge(right_summed, count(g, e))
                act.wait_ge(alpha_done, count(g, e))
                nc.scalar.activation(v_hi[:, e, :], vs_psum[:, e % 2, V0:V0 + D], ACT.Copy).then_inc(v_hi_done, 1)

            def exponentials(g, e):
                act.wait_ge(neg_max_done, count(g, e))
                nc.scalar.activation(exps[:, e, :], alpha[:, e, :], ACT.Exp, bias=neg_max[:, e:e + 1],
                                     accum_out=exp_sum[:, e:e + 1]).then_inc(exps_done, 1)

            def split_probs(g, e):
                act.wait_ge(inv_sum_done, count(g, e))
                nc.scalar.activation(probs_hi[:, e, :], exps[:, e, :], ACT.Copy,
                                     scale=inv_sum[:, e:e + 1]).then_inc(probs_hi_done, 1)

            for j in range(CH - 1):
                act.wait_ge(wqk_loaded[j + 1], 16)
                nc.scalar.activation(wqk_hi[:, j, :], wqk_raw[:, j + 1, :], ACT.Copy).then_inc(wqk_hi_done, 1)
            for c in range(CH):
                split_x(0, 0, c)
            for i, bank in enumerate(m_banks):
                act.wait_ge(m_summed, i + 1)
                nc.scalar.activation(m_hi[:, i, :], bank, ACT.Copy).then_inc(m_hi_done, 1)
            act.wait_ge(w_loaded, 16)
            for c in range(CH):
                nc.scalar.activation(moving_hi[:, c, 0:4, :], w_raw[:, c, :].rearrange("p (k n) -> p k n", n=P),
                                     ACT.Copy).then_inc(w_hi_done, 1)

            def phase(g, p, k):
                other = k
                if is_past(g):
                    return
                more = not (isinstance(g, int) and g + 1 >= GROUPS)
                for o in range(CH):
                    split_q(g, o)
                    if more and o < 2:
                        split_x(g + 1, other, 2 * o)
                        split_x(g + 1, other, 2 * o + 1)
                split_v(g, 0)
                exponentials(g, 0)
                split_probs(g, 0)
                for e in range(1, PACK):
                    exponentials(g, e)
                    split_probs(g, e)
                    split_v(g, e)

            over_groups(mybir.EngineType.Activation, phase)

        @block.gpsimd
        def _(pool):
            def split_x(g, slot, c):
                pool.wait_ge(x_hi_done, CH * g + c + 1)
                nc.gpsimd.tensor_tensor(x_lo[:, slot, c, :], xT_raw[:, c, :], f32(x_hi[:, slot, c, :]),
                                        ALU.subtract).then_inc(x_lo_done, 1)

            def inverse_deviation(g, e):
                pool.wait_ge(mean_var_done, count(g, e))
                nc.gpsimd.tensor_tensor(var_eps[:, e:e + 1], mean_var[:, e, 1:2], eps[:, :], ALU.add).then_inc(var_eps_done, 1)
                pool.wait_ge(var_eps_done, count(g, e))
                nc.gpsimd.tensor_tensor(rstd[:, e:e + 1], var_eps[:, e:e + 1], minus_half[:, :], ALU.pow).then_inc(rstd_done, 1)

            nc.gpsimd.memset(eps[:, :], EPS).then_inc(constants_set, 1)
            nc.gpsimd.memset(minus_half[:, :], -0.5).then_inc(constants_set, 1)
            pool.wait_ge(constants_set, 2)
            for c in range(CH):
                split_x(0, 0, c)

            def phase(g, p, k):
                behind, ahead = not is_first(g), not is_past(g)
                more = not (isinstance(g, int) and g + 1 >= GROUPS)
                if behind:
                    inverse_deviation(g - 1, 2)
                if more:
                    split_x(g + 1, k, 0)
                    split_x(g + 1, k, 1)
                if behind:
                    inverse_deviation(g - 1, 3)
                if more:
                    split_x(g + 1, k, 2)
                    split_x(g + 1, k, 3)
                if ahead:
                    inverse_deviation(g, 0)
                    inverse_deviation(g, 1)

            over_groups(mybir.EngineType.Pool, phase)

        @block.vector
        def _(dve):
            def make_mask(g, slot, loads):
                dve.wait_ge(adj_loaded[slot], 16 * loads)
                reached(dve, alpha_done, PACK * g)
                nc.vector.tensor_scalar(mask[:, :], adj[:, slot, :], 0.0, None, ALU.not_equal).then_inc(mask_done, 1)

            def split_q(g, o):
                dve.wait_ge(q_hi_done, CH * g + o + 1)
                nc.vector.tensor_tensor(moving_lo[:, o, 4:8, :], q_psum[:, o % 2, :].rearrange("p (e n) -> p e n", n=P),
                                        f32(moving_hi[:, o, 4:8, :]), ALU.subtract).then_inc(q_lo_done, 1)

            def split_v(g, e):
                dve.wait_ge(v_hi_done, count(g, e))
                nc.vector.tensor_tensor(v_lo[:, e, :], vs_psum[:, e % 2, V0:V0 + D], f32(v_hi[:, e, :]),
                                        ALU.subtract).then_inc(v_lo_done, 1)

            def mask_scores(g, e):
                if e == 0:
                    dve.wait_ge(mask_done, g + 1)
                dve.wait_ge(right_summed, count(g, e))
                nc.vector.scalar_tensor_tensor(alpha[:, e, :], vs_psum[:, e % 2, S0:S0 + P], 0.0,
                                               mask[:, e * P:(e + 1) * P], ALU.max, ALU.mult).then_inc(alpha_done, 1)
                dve.wait_ge(alpha_done, count(g, e))
                nc.vector.tensor_reduce(neg_max[:, e:e + 1], alpha[:, e, :], AX_X, ALU.max,
                                        negate=True).then_inc(neg_max_done, 1)

            def invert_sum(g, e):
                dve.wait_ge(exps_done, count(g, e))
                nc.vector.reciprocal(inv_sum[:, e:e + 1], exp_sum[:, e:e + 1]).then_inc(inv_sum_done, 1)

            def split_probs(g, e):
                dve.wait_ge(probs_hi_done, count(g, e))
                nc.vector.scalar_tensor_tensor(probs_lo[:, e, :], exps[:, e, :], inv_sum[:, e:e + 1],
                                               f32(probs_hi[:, e, :]), ALU.mult, ALU.subtract).then_inc(probs_lo_done, 1)

            def residual(g, slot, e, turn):
                if e == 0:
                    dve.wait_ge(rows_loaded[slot], 16 * (turn + 1))
                    reached(dve, y_stored[slot], 16 * turn)
                dve.wait_ge(out_summed, count(g, e))
                nc.vector.tensor_tensor(y[:, slot, e, :], out_psum[:, e % 2, :], x_rows[:, slot, e, :],
                                        ALU.add).then_inc(h_done, 1)

            def statistics(g, slot, e):
                dve.wait_ge(h_done, count(g, e))
                nc.vector.bn_stats(stats[:, e, :], y[:, slot, e, :]).then_inc(stats_done, 1)

            def await_statistics(g, e):
                dve.wait_ge(stats_done, count(g, e))

            def mean_variance(e):
                nc.vector.bn_aggr(mean_var[:, e, :], stats[:, e, :]).then_inc(mean_var_done, 1)

            def normalise(g, slot, e):
                dve.wait_ge(rstd_done, count(g, e))
                nc.vector.tensor_scalar(y[:, slot, e, :], y[:, slot, e, :], mean_var[:, e, 0:1], rstd[:, e:e + 1],
                                        ALU.subtract, ALU.mult).then_inc(y_done, 1)

            nc.vector.memset(warm[:, :], 0.0).then_inc(warm_set, 1)
            for j in range(CH - 1):
                dve.wait_ge(wqk_hi_done, j + 1)
                nc.vector.tensor_tensor(wqk_lo[:, j, :], wqk_raw[:, j + 1, :], f32(wqk_hi[:, j, :]),
                                        ALU.subtract).then_inc(wqk_lo_done, 1)
            for i, bank in enumerate(m_banks):
                dve.wait_ge(m_hi_done, i + 1)
                nc.vector.tensor_tensor(m_lo[:, i, :], bank, f32(m_hi[:, i, :]), ALU.subtract).then_inc(m_lo_done, 1)
            for c in range(CH):
                dve.wait_ge(w_hi_done, c + 1)
                nc.vector.tensor_tensor(moving_lo[:, c, 0:4, :], w_raw[:, c, :].rearrange("p (k n) -> p k n", n=P),
                                        f32(moving_hi[:, c, 0:4, :]), ALU.subtract).then_inc(w_lo_done, 1)

            def phase(g, p, k):
                slot, other = 1 - k, k
                behind, ahead = not is_first(g), not is_past(g)
                if behind:
                    residual(g - 1, other, 2, p)
                    statistics(g - 1, other, 2)
                    await_statistics(g - 1, 2)
                if ahead:
                    split_q(g, 0)
                if behind:
                    mean_variance(2)
                    residual(g - 1, other, 3, p)
                    statistics(g - 1, other, 3)
                    await_statistics(g - 1, 3)
                if ahead:
                    make_mask(g, slot, p + k + 1)
                if behind:
                    mean_variance(3)
                    normalise(g - 1, other, 2)
                if ahead:
                    split_q(g, 1)
                if behind:
                    normalise(g - 1, other, 3)
                if not ahead:
                    return
                split_q(g, 2)
                split_q(g, 3)

                mask_scores(g, 0)
                split_v(g, 0)
                invert_sum(g, 0)
                mask_scores(g, 1)
                split_probs(g, 0)
                invert_sum(g, 1)
                split_probs(g, 1)
                split_v(g, 1)
                for e in range(2, PACK):
                    mask_scores(g, e)
                    residual(g, slot, e - 2, p + k)
                    invert_sum(g, e)
                    statistics(g, slot, e - 2)
                    await_statistics(g, e - 2)
                    split_probs(g, e)
                    mean_variance(e - 2)
                    split_v(g, e)
                    normalise(g, slot, e - 2)

            over_groups(mybir.EngineType.DVE, phase)


def kernel(x, adj, L0_gnn_weight, L0_gnn_wq, L0_gnn_wk):
    import numpy as np
    import concourse.bacc as bacc
    from concourse.bass_utils import run_bass_kernel_spmd

    x, adj = np.asarray(x), np.asarray(adj)
    B, R, D = x.shape
    G, CH = B // PACK, D // P
    assert R == P and B % (2 * PACK) == 0
    xT = x.reshape(G, PACK, R, CH, P).transpose(0, 4, 3, 1, 2).reshape(G, P, CH * PACK * R)
    rows = x.reshape(G, PACK, R, D).transpose(0, 2, 1, 3).reshape(G, R, PACK * D)
    adjT = adj.reshape(G, PACK, R, R).transpose(0, 3, 1, 2).reshape(G, R, PACK * R)
    wqkT = np.concatenate([np.asarray(L0_gnn_wq).T.reshape(CH, P, D), np.asarray(L0_gnn_wk).T.reshape(CH, P, D)], axis=2)
    w = np.asarray(L0_gnn_weight).reshape(CH, P, D).transpose(1, 0, 2).reshape(P, CH * D)

    nc = bacc.Bacc("TRN2", target_bir_lowering=False, num_devices=1)
    arrays, args = {}, []
    for name, a in (("xT", xT), ("rows", rows), ("adjT", adjT), ("wqkT", wqkT), ("w", w)):
        arrays[name] = np.ascontiguousarray(a)
        args.append(nc.dram_tensor(name, a.shape, mybir.dt.from_np(a.dtype), kind="ExternalInput").ap())
    args.append(nc.dram_tensor("y_rows", (G, R, PACK * D), F32, kind="ExternalOutput").ap())
    graph_attention_layernorm(nc, *args)
    result = run_bass_kernel_spmd(nc, [arrays], core_ids=[0])
    y_rows = result.results[0]["y_rows"]
    return y_rows.reshape(G, R, PACK, D).transpose(0, 2, 1, 3).reshape(B, R, D)
```
